# Optimizing a Trainium2 kernel written in Bass

```python
import numpy as np
import jax
import jax.numpy as jnp

def _softmax(x, axis=-1):
    return jax.nn.softmax(x, axis=axis)

def _gelu(x):
    return jax.nn.gelu(x, approximate=True)

def _silu(x):
    return jax.nn.silu(x)

def _sigmoid(x):
    return jax.nn.sigmoid(x)

def _layernorm(x, axis=-1, eps=1e-05):
    m = jnp.mean(x, axis=axis, keepdims=True)
    v = jnp.var(x, axis=axis, keepdims=True)
    return (x - m) / jnp.sqrt(v + eps)

def _scatter_add(tgt, idx, src, axis=0):
    return tgt.at[idx].add(src)

def _segment_sum(src, seg, n):
    return jax.ops.segment_sum(src, seg, n)
kernel_name = 'mk_gnn_preln_d4_gnn_r32_2ffb07'

def setup_inputs(seed: int=0):
    np.random.seed(seed)
    _w = jnp.asarray

    def _rec_inputs():
        import jax
        import jax.numpy as jnp
        _gk = jax.random.key(seed)
        x = -0.0005121 + 1.001 * jax.random.normal(jax.random.fold_in(_gk, 1), (3125, 64), jnp.float32)
        _s = jax.random.randint(jax.random.fold_in(_gk, 2), (50000,), 0, 3125, jnp.int32)
        _d = jax.random.randint(jax.random.fold_in(_gk, 3), (50000,), 0, 3125, jnp.int32)
        _loop = jnp.arange(3125, dtype=jnp.int32)
        src = jnp.concatenate([_s, _d, _loop])
        dst = jnp.concatenate([_d, _s, _loop])
        _o = jnp.argsort(dst, stable=True)
        src = src[_o]
        dst = dst[_o]
        edge_type_16 = jax.random.randint(jax.random.fold_in(_gk, 12), (103125,), 0, 16, jnp.int32)
        edge_type_8 = jax.random.randint(jax.random.fold_in(_gk, 13), (103125,), 0, 8, jnp.int32)
        edge_weight1 = jax.random.uniform(jax.random.fold_in(_gk, 14), (103125, 1), jnp.float32, 0.0, 0.999998)
        node_type_4 = jax.random.randint(jax.random.fold_in(_gk, 15), (3125,), 0, 4, jnp.int32)
        return (x, src, dst, edge_type_16, edge_type_8, edge_weight1, node_type_4)
    x, src, dst, edge_type_16, edge_type_8, edge_weight1, node_type_4 = _rec_inputs()

    def _L0_gnn_setup():
        import jax, jax.numpy as jnp
        import numpy as np
        N, E, R, D_IN, D_OUT = (50000, 25000, 8, 64, 64)
        key = jax.random.key(seed)
        ks = jax.random.split(key, 8)
        feat = jax.random.normal(ks[0], (N, D_IN), dtype=jnp.float32)
        edge_src = jax.random.randint(ks[1], (E,), 0, N, dtype=jnp.int32)
        edge_dst = jax.random.randint(ks[2], (E,), 0, N, dtype=jnp.int32)
        etype = jax.random.randint(ks[3], (E,), 0, R, dtype=jnp.int32)
        attention = jax.random.uniform(ks[4], (E, 1), dtype=jnp.float32)
        weight = jax.random.normal(ks[5], (R, D_IN, D_OUT), dtype=jnp.float32) * (6.0 / (D_IN + D_OUT)) ** 0.5
        h_bias = jnp.zeros((D_OUT,), dtype=jnp.float32)
        loop_weight = jax.random.normal(ks[6], (D_IN, D_OUT), dtype=jnp.float32) * (6.0 / (D_IN + D_OUT)) ** 0.5
        return {'feat': feat, 'edge_src': edge_src, 'edge_dst': edge_dst, 'etype': etype, 'attention': attention, 'weight': weight, 'h_bias': h_bias, 'loop_weight': loop_weight}
    _L0_gnn_all = _L0_gnn_setup()
    _L0_gnn_in = {k: v for k, v in _L0_gnn_all.items() if k in ('weight', 'h_bias', 'loop_weight')}
    del _L0_gnn_all

    def _L1_gnn_setup():
        import jax, jax.numpy as jnp
        import numpy as np
        N_NODES = 3125
        N_EDGES = 100000
        IN_FEAT = 64
        OUT_FEAT = 64
        NUM_RELS = 16
        key = jax.random.key(seed)
        k1, k2, k3, k4, k5, k6 = jax.random.split(key, 6)
        h = jax.random.normal(k1, (N_NODES, IN_FEAT), dtype=jnp.float32)
        weight = jax.random.normal(k2, (NUM_RELS, IN_FEAT, OUT_FEAT), dtype=jnp.float32) * 0.1
        norm = jax.random.uniform(k3, (N_EDGES, 1), dtype=jnp.float32)
        src = jax.random.randint(k4, (N_EDGES,), 0, N_NODES, dtype=jnp.int32)
        dst = jax.random.randint(k5, (N_EDGES,), 0, N_NODES, dtype=jnp.int32)
        rel_type = jax.random.randint(k6, (N_EDGES,), 0, NUM_RELS, dtype=jnp.int32)
        return {'h': h, 'weight': weight, 'norm': norm, 'src': src, 'dst': dst, 'rel_type': rel_type}
    _L1_gnn_all = _L1_gnn_setup()
    _L1_gnn_in = {k: v for k, v in _L1_gnn_all.items() if k in ('weight',)}
    del _L1_gnn_all

    def _L2_gnn_setup():
        import jax, jax.numpy as jnp
        import numpy as np
        N_NODES = 3125
        N_EDGES = 50000
        D_IN = 64
        D_OUT = 64
        key = jax.random.key(seed)
        k1, k2, k3, k4, k5 = jax.random.split(key, 5)
        feat = jax.random.normal(k1, (N_NODES, D_IN), dtype=jnp.float32)
        weight1 = jax.random.normal(k2, (D_IN, D_OUT), dtype=jnp.float32) * (1.0 / np.sqrt(D_IN))
        weight2 = jax.random.normal(k3, (D_IN, D_OUT), dtype=jnp.float32) * (1.0 / np.sqrt(D_IN))
        src = jax.random.randint(k4, (N_EDGES,), 0, N_NODES, dtype=jnp.int32)
        dst = jax.random.randint(k5, (N_EDGES,), 0, N_NODES, dtype=jnp.int32)
        return {'feat': feat, 'weight1': weight1, 'weight2': weight2, 'src': src, 'dst': dst}
    _L2_gnn_all = _L2_gnn_setup()
    _L2_gnn_in = {k: v for k, v in _L2_gnn_all.items() if k in ('weight1', 'weight2')}
    del _L2_gnn_all

    def _L3_gnn_setup():
        import jax, jax.numpy as jnp
        import numpy as np
        N, E = (1250, 20000)
        IN, H, HS = (64, 4, 16)
        NT, ET = (4, 8)

        def typed_linear(x, W, types):
            out = jnp.zeros((x.shape[0], W.shape[-1]), x.dtype)
            for t in range(W.shape[0]):
                out = out + jnp.where((types == t)[:, None], x @ W[t], 0.0)
            return out

        def typed_head_linear(z, W, types):
            out = jnp.zeros_like(z)
            for t in range(W.shape[1]):
                out = out + jnp.where((types == t)[:, None, None], jnp.einsum('ehd,hdo->eho', z, W[:, t]), 0.0)
            return out
        key = jax.random.key(seed)
        ks = jax.random.split(key, 12)
        x = jax.random.normal(ks[0], (N, IN), jnp.float32)
        ntype = jax.random.randint(ks[1], (N,), 0, NT)
        etype = jax.random.randint(ks[2], (E,), 0, ET)
        src = jax.random.randint(ks[3], (E,), 0, N)
        dst = jax.random.randint(ks[4], (E,), 0, N)
        s_in = 1.0 / np.sqrt(IN).astype(np.float32)
        s_hs = 1.0 / np.sqrt(HS).astype(np.float32)
        s_m = 1.0 / np.sqrt(H * HS).astype(np.float32)
        Wk = jax.random.normal(ks[5], (NT, IN, H * HS), jnp.float32) * s_in
        Wq = jax.random.normal(ks[6], (NT, IN, H * HS), jnp.float32) * s_in
        Wv = jax.random.normal(ks[7], (NT, IN, H * HS), jnp.float32) * s_in
        Wa = jax.random.normal(ks[8], (NT, H * HS, H * HS), jnp.float32) * s_m
        rel_att = jax.random.normal(ks[9], (H, ET, HS, HS), jnp.float32) * s_hs
        rel_msg = jax.random.normal(ks[10], (H, ET, HS, HS), jnp.float32) * s_hs
        rel_pri = jnp.ones((H, ET), jnp.float32)
        return {'x': x, 'ntype': ntype, 'etype': etype, 'src': src, 'dst': dst, 'Wk': Wk, 'Wq': Wq, 'Wv': Wv, 'Wa': Wa, 'rel_att': rel_att, 'rel_msg': rel_msg, 'rel_pri': rel_pri}
    _L3_gnn_all = _L3_gnn_setup()
    _L3_gnn_in = {k: v for k, v in _L3_gnn_all.items() if k in ('Wk', 'Wq', 'Wv', 'Wa', 'rel_att', 'rel_msg', 'rel_pri')}
    del _L3_gnn_all
    return {'x': x, 'src': src, 'dst': dst, 'edge_type_16': edge_type_16, 'edge_type_8': edge_type_8, 'edge_weight1': edge_weight1, 'node_type_4': node_type_4, 'L0_gnn_weight': _L0_gnn_in['weight'], 'L0_gnn_h_bias': _L0_gnn_in['h_bias'], 'L0_gnn_loop_weight': _L0_gnn_in['loop_weight'], 'L1_gnn_weight': _L1_gnn_in['weight'], 'L2_gnn_weight1': _L2_gnn_in['weight1'], 'L2_gnn_weight2': _L2_gnn_in['weight2'], 'L3_gnn_Wk': _L3_gnn_in['Wk'], 'L3_gnn_Wq': _L3_gnn_in['Wq'], 'L3_gnn_Wv': _L3_gnn_in['Wv'], 'L3_gnn_Wa': _L3_gnn_in['Wa'], 'L3_gnn_rel_att': _L3_gnn_in['rel_att'], 'L3_gnn_rel_msg': _L3_gnn_in['rel_msg'], 'L3_gnn_rel_pri': _L3_gnn_in['rel_pri']}

def reference(x, src, dst, edge_type_16, edge_type_8, edge_weight1, node_type_4, L0_gnn_weight, L0_gnn_h_bias, L0_gnn_loop_weight, L1_gnn_weight, L2_gnn_weight1, L2_gnn_weight2, L3_gnn_Wk, L3_gnn_Wq, L3_gnn_Wv, L3_gnn_Wa, L3_gnn_rel_att, L3_gnn_rel_msg, L3_gnn_rel_pri):
    import jax
    import jax.numpy as jnp

    def _L0_gnn_ref(feat, edge_src, edge_dst, etype, attention, weight, h_bias, loop_weight):
        import jax, jax.numpy as jnp
        import numpy as np
        N, E, R, D_IN, D_OUT = (50000, 25000, 8, 64, 64)
        proj = jnp.einsum('ni,rio->rno', feat, weight)
        m = (proj[etype, edge_src] + h_bias) * attention
        agg = jax.ops.segment_sum(m, edge_dst, num_segments=feat.shape[0])
        return agg + feat @ loop_weight

    def _L1_gnn_ref(h, weight, norm, src, dst, rel_type):
        import jax, jax.numpy as jnp
        import numpy as np
        N_NODES = 3125
        N_EDGES = 100000
        IN_FEAT = 64
        OUT_FEAT = 64
        NUM_RELS = 16
        n_nodes = h.shape[0]
        transformed = jnp.einsum('nd,rdo->nro', h, weight)
        msg = transformed[src, rel_type] * norm
        agg = jax.ops.segment_sum(msg, dst, num_segments=n_nodes)
        return jax.nn.relu(agg)

    def _L2_gnn_ref(feat, weight1, weight2, src, dst):
        import jax, jax.numpy as jnp
        import numpy as np
        N_NODES = 3125
        N_EDGES = 50000
        D_IN = 64
        D_OUT = 64
        N = feat.shape[0]
        ones_e = jnp.ones(src.shape[0], dtype=feat.dtype)
        out_deg = jnp.clip(jax.ops.segment_sum(ones_e, src, num_segments=N), 1.0)
        feat_n = feat * jax.lax.rsqrt(out_deg)[:, None]
        h_src = feat_n[src]
        copy_sum = jax.ops.segment_sum(h_src, dst, num_segments=N)
        inner_sum = jax.ops.segment_sum(h_src * feat_n[dst], dst, num_segments=N)
        rst = copy_sum @ weight1 + inner_sum @ weight2
        in_deg = jnp.clip(jax.ops.segment_sum(ones_e, dst, num_segments=N), 1.0)
        rst = rst * jax.lax.rsqrt(in_deg)[:, None]
        return rst

    def _L3_gnn_ref(x, ntype, etype, src, dst, Wk, Wq, Wv, Wa, rel_att, rel_msg, rel_pri):
        import jax, jax.numpy as jnp
        import numpy as np
        N, E = (1250, 20000)
        IN, H, HS = (64, 4, 16)
        NT, ET = (4, 8)

        def typed_linear(x, W, types):
            out = jnp.zeros((x.shape[0], W.shape[-1]), x.dtype)
            for t in range(W.shape[0]):
                out = out + jnp.where((types == t)[:, None], x @ W[t], 0.0)
            return out

        def typed_head_linear(z, W, types):
            out = jnp.zeros_like(z)
            for t in range(W.shape[1]):
                out = out + jnp.where((types == t)[:, None, None], jnp.einsum('ehd,hdo->eho', z, W[:, t]), 0.0)
            return out
        n = x.shape[0]
        h_heads, hs = (rel_att.shape[0], rel_att.shape[-1])
        sqrt_d = jnp.asarray(np.sqrt(hs), x.dtype)
        k = typed_linear(x, Wk, ntype).reshape(n, h_heads, hs)
        q = typed_linear(x, Wq, ntype).reshape(n, h_heads, hs)
        v = typed_linear(x, Wv, ntype).reshape(n, h_heads, hs)
        ke, qe, ve = (k[src], q[dst], v[src])
        kw = typed_head_linear(ke, rel_att, etype)
        qw = typed_head_linear(qe, rel_att, etype)
        a = (kw * qw).sum(-1) * rel_pri[:, etype].T / sqrt_d
        m = typed_head_linear(ve, rel_msg, etype)
        amax = jax.ops.segment_max(a, dst, num_segments=n)
        ex = jnp.exp(a - amax[dst])
        denom = jax.ops.segment_sum(ex, dst, num_segments=n)
        alpha = ex / denom[dst]
        h = jax.ops.segment_sum(m * alpha[:, :, None], dst, num_segments=n)
        h = h.reshape(n, h_heads * hs)
        return typed_linear(h, Wa, ntype)
    h = jnp.maximum(_layernorm(x, axis=-1), 0.0)
    x = x + _L0_gnn_ref(h, src, dst, edge_type_8, edge_weight1, L0_gnn_weight, L0_gnn_h_bias, L0_gnn_loop_weight)
    h = jnp.maximum(_layernorm(x, axis=-1), 0.0)
    x = x + _L1_gnn_ref(h, L1_gnn_weight, edge_weight1, src, dst, edge_type_16)
    h = jnp.maximum(_layernorm(x, axis=-1), 0.0)
    x = x + _L2_gnn_ref(h, L2_gnn_weight1, L2_gnn_weight2, src, dst)
    h = jnp.maximum(_layernorm(x, axis=-1), 0.0)
    x = x + _L3_gnn_ref(h, node_type_4, edge_type_8, src, dst, L3_gnn_Wk, L3_gnn_Wq, L3_gnn_Wv, L3_gnn_Wa, L3_gnn_rel_att, L3_gnn_rel_msg, L3_gnn_rel_pri)
    return x

_drawn_inputs = setup_inputs


def setup_inputs(seed=0):
    import zlib

    import numpy as np

    out = dict(_drawn_inputs(seed))
    spreads = {'L0_gnn_h_bias': (0.0, 0.1), 'L3_gnn_rel_pri': (1.0, 0.6)}
    factors = {'L2_gnn_weight2': 2.76, 'L3_gnn_Wk': 3.324, 'L3_gnn_Wq': 3.085, 'L3_gnn_rel_att': 3.793}
    for name, (base, spread) in spreads.items():
        noise = np.random.default_rng([zlib.crc32(name.encode()), seed]).standard_normal(out[name].shape)
        drawn = base * np.exp(spread * noise) if base else spread * noise
        out[name] = jnp.asarray(drawn.astype(out[name].dtype))
    for name, factor in factors.items():
        out[name] = (out[name] * factor).astype(out[name].dtype)
    return out
```

```python
from contextlib import ExitStack

import concourse.bass as bass
from concourse import mybir

P = 128
F32 = mybir.dt.float32
BF16 = mybir.dt.bfloat16
I32 = mybir.dt.int32
ALU = mybir.AluOpType
ACT = mybir.ActivationFunctionType
AX_X = mybir.AxisListType.X

N = 3125
E = 103125
D = 64
NW = -(-N // P)
NP = NW * P
NB = NW + 1
EC = -(-E // P)
LASTP = E - (P - 1) * EC
LASTN = N - (NW - 1) * P
T = 832
assert T >= EC + NW and T % 32 == 0
REC = 4
RB = 31
assert EC % (2 * RB) == 0
G = 16
G3 = 8
AW = 68
WPB = 7
BANK = 512
SCRATCH = 17 * T
ACC_BANKS = -(-NW // WPB)
R0, R1, R3 = 8, 16, 8
NT = 4
H, HS = 4, 16
EPS = 1e-5
FAR = 1.0e30


def acc_at(w):
    return (w // WPB) * BANK + (w % WPB) * AW


class Steps:

    def __init__(self, engine, sem):
        self.engine, self.sem, self.done, self.at, self.per = engine, sem, 0, None, 0

    def after(self, instruction):
        instruction.then_inc(self.sem, 1)
        self.done += 1
        now = self.done if self.at is None else self.at * self.per + self.done
        self.engine.wait_ge(self.sem, now)

    def enter(self, index, per, first=0):
        self.at, self.per, self.entered = index, per, self.done
        self.done -= first * per

    def leave(self, turns, first=0):
        assert self.done + first * self.per - self.entered == self.per, (self.done, self.entered, self.per)
        self.at, self.done = None, self.entered + self.per * turns


class Group:

    def __init__(self, turn, half):
        self.turn, self.half, self.n = turn, half, turn * 2 + half

    def next(self):
        return Group(self.turn + self.half, 1 - self.half)

    def prev(self):
        return Group(self.turn - (1 - self.half), 1 - self.half)

    def second(self):
        return isinstance(self.n, int) and self.n == 1


def gnn_kernel(nc, x, src, dst, edge_type_16, edge_type_8, edge_weight1, node_type_4, w0, bias0,
               loop0, w1, w2a, w2b, wk, wq, wv, wa, rel_att, rel_msg, rel_pri, out, layers=4):
    table0 = nc.dram_tensor("table0", [NP * R0, D], F32, kind="Internal").ap()
    table1 = nc.dram_tensor("table1", [NP * R1, D], F32, kind="Internal").ap()
    table2 = nc.dram_tensor("table2", [NP, D], F32, kind="Internal").ap()
    table3 = nc.dram_tensor("table3", [NP * R3, 2 * D], F32, kind="Internal").ap()
    records = nc.dram_tensor("records", [T * P, REC], I32, kind="Internal").ap()
    messages = nc.dram_tensor("messages", [T // G3, P, G3 * D], F32, kind="Internal").ap()

    with ExitStack() as ctx:
        def sb(name, shape, dt=F32):
            return ctx.enter_context(nc.sbuf_tensor(name, shape, dt))

        def sem(name):
            return ctx.enter_context(nc.semaphore(name))

        acc = ctx.enter_context(nc.psum_tensor("acc", [P, ACC_BANKS * BANK], F32))
        work = ctx.enter_context(nc.psum_tensor("work", [P, 4 * BANK], F32))

        def bank(i):
            return work[:, i * BANK:(i + 1) * BANK]

        ident = sb("ident", [P, P])
        identb = sb("identb", [P, P], BF16)
        before = sb("before", [P, P])
        ones = sb("ones", [P, P])
        iota = sb("iota", [P, T])
        iotab = sb("iotab", [P, P], BF16)
        part_i = sb("part_i", [P, 1], I32)
        part = sb("part", [P, 1])
        zeros = sb("zeros", [P, BANK], BF16)
        half = sb("half", [P, 2])

        xs = sb("xs", [P, NW, D])
        hs = sb("hs", [P, NW, D])
        cs = sb("cs", [P, NW, D])
        stat = sb("stat", [P, 4, NW])
        hist = sb("hist", [P, 2, NW])

        recs = sb("recs", [P, T, REC], I32)
        row8 = sb("row8", [P, T], I32)
        row16 = sb("row16", [P, T], I32)
        local = sb("local", [P, T])
        weight = sb("weight", [P, T])
        winrow = sb("winrow", [P, T])
        acc_off = sb("acc_off", [P, T], I32)
        q_off = sb("q_off", [P, T], I32)
        start_i = sb("start_i", [P, T], I32)
        iota_i = q_off
        digits = sb("digits", [P, 4 * T])
        src_lo, src_hi, dst_lo, dst_hi = (digits[:, i * T:(i + 1) * T] for i in range(4))
        tile_max = digits

        scratch = sb("scratch", [P, SCRATCH])
        spos = [0]

        def cut(n, dt=F32):
            a = scratch[:, spos[0]:spos[0] + n]
            spos[0] += n
            assert spos[0] <= SCRATCH
            return a.bitcast(dt) if dt != F32 else a

        raw_src, raw_dst, raw_t16, raw_t8 = (cut(EC, I32) for _ in range(4))
        raw_w = cut(EC)
        win_i = cut(EC, I32)
        win = cut(EC)
        isb = cut(EC)
        cum = cum_ = cut(EC)
        picked = cut(EC)
        pos = cut(EC)
        pos_i = cut(EC, I32)
        recs_in = cut(EC * REC, I32).rearrange("p (c r) -> p c r", r=REC)
        far_edges = cut((T - EC) * REC, I32).rearrange("p (c r) -> p c r", r=REC)
        spos[0] = 0
        hT2 = cut(NP)
        typeT = cut(NP)
        hm = [cut(NP), cut(NP)]
        assert spos[0] <= SCRATCH
        types_i = hm[1].bitcast(I32)
        twice = hm[0].rearrange("p (w c) -> p w c", c=P)
        kvT = sb("kvT", [P, NP])
        qn = sb("qn", [P, NW * D])
        hT = kvT

        totals = sb("totals", [P, NB])
        offs = sb("offs", [P, NB])
        cur = sb("cur", [P, 2])
        small = sb("small", [P, 8])
        small_i = sb("small_i", [P, 2], I32)
        geq = sb("geq", [P, T])
        deltab = sb("deltab", [P, P])

        w0_sb = sb("w0_sb", [D, R0, D])
        w1_sb = sb("w1_sb", [D, R1, D])
        loop_sb = sb("loop_sb", [D, D])
        bias_sb = sb("bias_sb", [P, D])
        w2_sb = sb("w2_sb", [P, D])
        wkv_sb = sb("wkv_sb", [P, 2, P])
        wq_sb = sb("wq_sb", [P, 2, D])
        wa_sb = sb("wa_sb", [P, 2, D])
        attT = sb("attT", [D, R3, D])
        rel3 = sb("rel3", [P, R3, P])
        pri = sb("pri", [D, R3])
        att = sb("att", [D, R3, D])

        stage_row = [sb(f"stage_row{i}", [P, RB], I32) for i in range(2)]
        stage_rec = [sb(f"stage_rec{i}", [P, RB, REC], I32) for i in range(2)]
        stage_f = [sb(f"stage_f{i}", [P, 4, G]) for i in range(2)]
        spos[0] = 0
        hot = [cut(G * P).rearrange("p (g d) -> p g d", d=P) for i in range(2)]
        hotb = [cut(G * P // 2, BF16).rearrange("p (g d) -> p g d", d=P) for i in range(2)]
        hot_hi = [cut(G * NW // 2, BF16).rearrange("p (g d) -> p g d", d=NW) for i in range(2)]
        ring = cut(2 * G * AW).rearrange("p (h g c) -> p h g c", h=2, c=AW)
        spos[0] = 0

        def tiles3(cols, dt=F32):
            a = cut(G3 * cols // (2 if dt == BF16 else 1), dt)
            return a.rearrange("p (g c) -> p g c", c=cols)

        rows3 = [tiles3(2 * D) for i in range(2)]
        hot3 = [tiles3(P) for i in range(2)]
        hot3b = [tiles3(P, BF16) for i in range(2)]
        hotT = [tiles3(P) for i in range(2)]
        far = tiles3(P, BF16)
        prod = tiles3(D)
        msg_in = [tiles3(D) for i in range(2)]
        msg = [tiles3(AW) for i in range(2)]
        fwd = scratch[:, 0:T * H]
        change = scratch[:, T * H:T * H + 2 * T].rearrange("p (a t) -> p a t", a=2)
        score = recs[:, :, :].rearrange("p t r -> p (t r)").bitcast(F32)
        a_g = sb("a_g", [P, 3, G3 * H])
        a_parts = sb("a_parts", [P, 3, G3 * H], BF16)
        partsT = [sb(f"partsT{i}", [3 * G3 * H, P], BF16) for i in range(2)]
        sel = sb("sel", [3 * G3 * H, G3 * H], BF16)
        max_g = sb("max_g", [P, G3, H])
        diff = [sb(f"diff{i}", [P, G3 * H]) for i in range(2)]
        den = sb("den", [P, NW, H])
        evac = [sb(f"evac{i}", [P, 2 * BANK]) for i in range(2)]

        s_dve, s_pool = sem("s_dve"), sem("s_pool")
        pool_held, pe_held, dve_held = sem("pool_held"), sem("pe_held"), sem("dve_held")

        s_edges = sem("s_edges")
        s_nodes = sem("s_nodes")
        s_weights = sem("s_weights")
        s_clear = sem("s_clear")
        s_const = sem("s_const")
        s_totals = sem("s_totals")
        s_off = sem("s_off")
        s_cnt = sem("s_cnt")
        s_tiles = sem("s_tiles")
        s_geq = sem("s_geq")
        s_win = sem("s_win")
        s_starts = sem("s_starts")
        s_far = sem("s_far")
        s_recst = sem("s_recst")
        s_recout = [sem(f"s_recout{i}") for i in range(2)]
        s_sorted = sem("s_sorted")
        s_recs = [sem(f"s_recs{i}") for i in range(2)]

        s_clear3 = sem("s_clear3")
        s_weights3 = sem("s_weights3")
        s_types = sem("s_types")
        s_free3 = sem("s_free3")
        s_attp, s_attT, s_relp, s_rel = sem("s_attp"), sem("s_attT"), sem("s_relp"), sem("s_rel")
        s_hm = sem("s_hm")
        s_kvp, s_kv = sem("s_kvp"), sem("s_kv")
        s_qp, s_qn = sem("s_qp"), sem("s_qn")
        s_outp, s_outx = sem("s_outp"), sem("s_outx")

        block = ctx.enter_context(nc.Block())

        class Layer:

            def __init__(self, n):
                self.norm = sem(f"l{n}_norm")
                self.turned = sem(f"l{n}_turned")
                self.turned_sb = sem(f"l{n}_turned_sb")
                self.made = sem(f"l{n}_made")
                self.taken = sem(f"l{n}_taken")
                self.stored = [sem(f"l{n}_stored{i}") for i in range(2)]
                self.staged = sem(f"l{n}_staged")
                self.gathered = [sem(f"l{n}_gathered{i}") for i in range(2)]
                if n < 3:
                    self.scal = sem(f"l{n}_scal")
                    self.hots = sem(f"l{n}_hots")
                    self.summed = sem(f"l{n}_summed")
                self.done = sem(f"l{n}_done")

        L = [Layer(n) for n in range(4)]

        class Loop3:

            def __init__(self, n):
                self.hots = sem(f"p{n}_hots")
                self.tp = sem(f"p{n}_tp")
                self.hotT = sem(f"p{n}_hotT")
                self.picked = sem(f"p{n}_picked")
                self.used = sem(f"p{n}_used")
                self.scal = sem(f"p{n}_scal")

        P1, P2 = Loop3(1), Loop3(2)
        s_free = [sem(f"s_free{i}") for i in range(2)]
        s_spill = [sem(f"s_spill{i}") for i in range(2)]
        s_parts = sem("s_parts")
        s_partsp, s_partsT = sem("s_partsp"), sem("s_partsT")
        s_farm = sem("s_farm")
        s_mx, s_red = sem("s_mx"), sem("s_red")
        s_maxima = sem("s_maxima")
        s_msg_in = [sem(f"s_msg_in{i}") for i in range(2)]
        s_diff, s_exp = sem("s_diff"), sem("s_exp")
        s_msg = sem("s_msg")
        s_sum = sem("s_sum")
        HALF_T = T // 2
        W3 = 8 + 3 * H
        NG3 = T // G3
        assert NG3 % 2 == 0
        TURNS = T // (2 * G)

        s_final, s_out = sem("s_final"), sem("s_out")
        s_var, s_std = sem("s_var"), sem("s_std")
        s_deg, s_degroot = sem("s_deg"), sem("s_degroot")
        s_taken_acc, s_identb = sem("s_taken_acc"), sem("s_identb")
        s_cat, s_catT, s_catp, s_comb, s_added = sem("s_cat"), sem("s_catT"), sem("s_catp"), sem("s_comb"), sem("s_added")

        def store_table(sp, lay, table, width):
            rows = table.rearrange("(w p r) d -> w p (r d)", p=P, r=width // table.shape[1])
            for w in range(NW):
                sp.wait_ge(lay.taken, w + 1)
                sp.dma_start(rows[w], evac[w % 2][:, 0:width]).then_inc(lay.stored[w % 2], 16)

        def finish(sp):
            sp.wait_ge(s_final, 1)
            sp.dma_start(out[0:(NW - 1) * P, :].rearrange("(w p) d -> p w d", p=P), xs[:, 0:NW - 1, :]).then_inc(s_out, 16)
            sp.dma_start(out[(NW - 1) * P:N, :], xs[0:LASTN, NW - 1, :]).then_inc(s_out, 16)
            sp.wait_ge(s_out, 32)

        def load_tiles(eng, part_of):
            with eng.Fori(0, HALF_T // 8) as it:
                at = it * 8 + part_of * HALF_T
                _, starts = nc.values_load_multi_w_load_instructions(
                    start_i[0:1, bass.ds(at, 8)], engines=[eng.engine], min_val=0, max_val=(T - 1) * P,
                    skip_runtime_bounds_check_because="starts are sums of counts of edges")
                for k in range(8):
                    eng.dma_start(recs[:, bass.ds(at + k, 1), :].rearrange("p o r -> p (o r)"),
                                  records[bass.ds(starts[k], P), :]).then_inc(s_recs[part_of], 16)

        def node_act(act, k):
            act.wait_ge(s_var, k + 1)
            nc.scalar.activation(stat[:, 2, :], stat[:, 1, :], ACT.Sqrt).then_inc(s_std, 1)
            if k == 2:
                act.wait_ge(s_deg, 1)
                nc.scalar.activation(stat[:, 3, :], hist[:, 0, :], ACT.Sqrt).then_inc(s_degroot, 1)
                nc.scalar.activation(stat[:, 2, :], hist[:, 1, :], ACT.Sqrt).then_inc(s_degroot, 1)

        def gather_rows(pool, k):
            lay = L[k]
            table = (table0, table1, table2)[k]
            for i in range(2):
                n = 1 if k == 2 else (NW + 1 - i) // 2
                if k != 2 or i == 0:
                    pool.wait_ge(lay.stored[i], 16 * n)
            with pool.Fori(0, TURNS) as it:
                for h in range(2):
                    pool.wait_ge(lay.staged, it * 2 + (h + 1))
                    pool.sem_inc(pool_held, 1)
                    for j in range(G):
                        pool.indirect_dma_start(ring[:, h, j, 0:D], None, table,
                                                bass.IndirectOffsetOnAxis(stage_row[h][:, j:j + 1], 0)).then_inc(lay.gathered[h], 16)

        def turn_pe(pe, lay, n_rows, source):
            for w in range(NW):
                if w % 4 == 0 and w >= 8:
                    pe.wait_ge(lay.turned_sb, w // 4 - 1)
                last = nc.tensor.transpose(bank((w // 4) % 2)[0:n_rows, (w % 4) * P:(w % 4 + 1) * P], source(w), ident[:, :])
                if w % 4 == 3 or w == NW - 1:
                    last.then_inc(lay.turned, 1)

        def node_pe(pe, k):
            lay = L[k]
            if k > 0:
                pe.wait_ge(s_taken_acc, k)
            else:
                pe.wait_ge(s_identb, 1)
            for b in range(ACC_BANKS):
                last = nc.tensor.matmul(acc[:, b * BANK:(b + 1) * BANK], identb[:, :], zeros[:, :], start=True, stop=False, skip_group_check=True)
            if k == 2:
                return
            pe.wait_ge(lay.norm, 1)
            turn_pe(pe, lay, D, lambda w: hs[:, w, :])
            wts = (w0_sb, w1_sb)[k]
            R = (R0, R1)[k]
            pe.wait_ge(s_weights, 16 * 6)
            for w in range(NW):
                pe.wait_ge(lay.turned_sb, w // 4 + 1)
                if w == 0:
                    pe.wait_ge(lay.turned_sb, -(-NW // 4))
                if w >= 2:
                    pe.wait_ge(lay.taken, w - 1)
                lhsT = hT[0:D, w * P:(w + 1) * P]
                for c in range(R * D // BANK):
                    last = nc.tensor.matmul(bank((w % 2) * 2 + c), lhsT, wts[:, c * 8:(c + 1) * 8, :].rearrange("i r o -> i (r o)"), start=True, stop=True)
                last.then_inc(lay.made, 1)
                if k == 0:
                    nc.tensor.matmul(acc[:, acc_at(w):acc_at(w) + D], lhsT, loop_sb[:, :], start=False, stop=False, skip_group_check=True)

        def edge_pe(pe, k):
            lay = L[k]
            pe.sem_inc(lay.summed, 2)
            if k < 2:
                pe.wait_ge(lay.taken, NW)
                nc.tensor.matmul(work[:, 0:BANK], identb[:, :], zeros[:, :], start=True, stop=False, skip_group_check=True)
            with pe.Fori(0, TURNS) as it:
                for h in range(2):
                    at = it * (2 * G) + h * G
                    _, offs_ = nc.values_load_multi_w_load_instructions(
                        acc_off[0:1, bass.ds(at, G)], engines=[pe.engine], min_val=0, max_val=acc_at(NW - 1),
                        skip_runtime_bounds_check_because="tiles' windows are below NW")
                    pe.wait_ge(lay.hots, it * 2 + (h + 1))
                    pe.sem_inc(pe_held, 1)
                    pe.wait_ge(lay.gathered[h], (it + 1) * (16 * G))
                    pe.sem_inc(pe_held, 1)
                    for j in range(G):
                        last = nc.tensor.matmul(acc[:, bass.ds(offs_[j], D)], hot[h][:, j, :], ring[:, h, j, 0:D],
                                                start=False, stop=False, skip_group_check=True)
                        if k < 2:
                            last = nc.tensor.matmul(work[:, k * NW:(k + 1) * NW], hotb[h][:, j, :], hot_hi[h][:, j, :],
                                                    start=False, stop=False, skip_group_check=True)
                    last.then_inc(lay.summed, 1)
            for b in range(ACC_BANKS):
                last = nc.tensor.matmul(acc[:, b * BANK:b * BANK + 1], identb[:, :], zeros[:, 0:1], start=False, stop=True, skip_group_check=True)
            last.then_inc(lay.done, 1)

        def combine_pe(pe):
            lay = L[2]
            pe.wait_ge(s_cat, 1)
            for w in range(NW):
                if w >= 2:
                    pe.wait_ge(s_catT, w - 1)
                nc.tensor.transpose(bank(w % 2)[:, 0:P], catn(w), ident[:, :]).then_inc(s_catp, 1)
                if w >= 1:
                    combine_one(pe, w - 1)
            combine_one(pe, NW - 1)

        def combine_one(pe, w):
            pe.wait_ge(s_catT, w + 1)
            if w >= 2:
                pe.wait_ge(s_added, w - 1)
            nc.tensor.matmul(bank(2 + w % 2)[:, 0:D], kvT[:, w * P:(w + 1) * P], w2_sb[:, :], start=True, stop=True).then_inc(s_comb, 1)

        cat = scratch[:, 0:NW * P].rearrange("p (w c) -> p w c", c=P)

        def catn(w):
            return cat[:, w, :]

        def norm_dve(dve, steps, k):
            after = steps.after

            def wide(a):
                return a.unsqueeze(2).broadcast_to([P, NW, D])

            after(nc.vector.tensor_reduce(stat[:, 0, :], xs[:, :, :], AX_X, ALU.add))
            after(nc.vector.tensor_scalar(stat[:, 0, :], stat[:, 0, :], 1.0 / D, None, ALU.mult))
            after(nc.vector.tensor_tensor(cs[:, :, :], xs[:, :, :], wide(stat[:, 0, :]), ALU.subtract))
            after(nc.vector.tensor_tensor(hs[:, :, :], cs[:, :, :], cs[:, :, :], ALU.mult))
            after(nc.vector.tensor_reduce(stat[:, 1, :], hs[:, :, :], AX_X, ALU.add))
            after(nc.vector.tensor_scalar(stat[:, 1, :], stat[:, 1, :], 1.0 / D, EPS, ALU.mult, ALU.add))
            dve.sem_inc(s_var, 1)
            dve.wait_ge(s_std, k + 1)
            after(nc.vector.reciprocal(stat[:, 2, :], stat[:, 2, :]))
            after(nc.vector.tensor_tensor(hs[:, :, :], cs[:, :, :], wide(stat[:, 2, :]), ALU.mult))
            after(nc.vector.tensor_scalar(hs[:, :, :], hs[:, :, :], 0.0, None, ALU.max))
            if k < 2:
                dve.sem_inc(L[k].norm, 1)

        def table_dve(dve, steps, k):
            lay = L[k]
            for g in range(-(-NW // 4)):
                n = min(4, NW - 4 * g) * P
                dve.wait_ge(lay.turned, g + 1)
                nc.vector.tensor_copy(hT[0:D, g * 4 * P:g * 4 * P + n], bank(g % 2)[0:D, 0:n]).then_inc(lay.turned_sb, 1)
            R = (R0, R1)[k]
            for w in range(NW):
                dve.wait_ge(lay.made, w + 1)
                if w >= 2:
                    dve.wait_ge(lay.stored[w % 2], 16 * (w // 2))
                o = evac[w % 2][:, 0:R * D]
                i = work[:, (w % 2) * 2 * BANK:(w % 2) * 2 * BANK + R * D]
                if k == 0:
                    nc.vector.tensor_tensor(o.rearrange("p (r d) -> p r d", d=D), i.rearrange("p (r d) -> p r d", d=D),
                                            bias_sb[:, :].unsqueeze(1).broadcast_to([P, R, D]), ALU.add).then_inc(lay.taken, 1)
                else:
                    nc.vector.tensor_copy(o, i).then_inc(lay.taken, 1)

        def degrees_dve(dve, steps):
            after = steps.after
            after(nc.vector.tensor_scalar(hist[:, :, :].rearrange("p a w -> p (a w)"), work[:, 2 * NW:4 * NW], 1.0, None, ALU.max) if False else
                  nc.vector.tensor_scalar(hist[:, :, :].rearrange("p a w -> p (a w)"), hcount[:, :], 1.0, None, ALU.max))
            dve.sem_inc(s_deg, 1)
            dve.wait_ge(s_degroot, 2)
            after(nc.vector.reciprocal(hist[:, 0, :], stat[:, 3, :]))
            after(nc.vector.reciprocal(hist[:, 1, :], stat[:, 2, :]))
            after(nc.vector.tensor_tensor(hs[:, :, :], hs[:, :, :], hist[:, 0, :].unsqueeze(2).broadcast_to([P, NW, D]), ALU.mult))
            after(nc.vector.tensor_scalar(row16[:, :], row8[:, :], 3, None, ALU.arith_shift_right))
            dve.sem_inc(L[2].norm, 1)

        hcount = sb("hcount", [P, 2 * NW])

        def edge_dve(dve, steps, k):
            lay = L[k]
            rows = (row8, row16, row16)[k]
            with dve.Fori(0, TURNS) as it:
                for h in range(2):
                    at = it * (2 * G) + h * G
                    dve.wait_ge(lay.summed, it * 2 + (h + 1))
                    dve.sem_inc(dve_held, 1)
                    nc.vector.tensor_copy(stage_row[h][:, 0:G], rows[:, bass.ds(at, G)]).then_inc(lay.staged, 1)
                    if k < 2:
                        nc.vector.tensor_copy(stage_f[h][:, 1, :], weight[:, bass.ds(at, G)])
                        nc.vector.tensor_copy(stage_f[h][:, 2, :], (src_lo, dst_lo)[k][:, bass.ds(at, G)])
                        nc.vector.tensor_copy(stage_f[h][:, 3, :], (src_hi, dst_hi)[k][:, bass.ds(at, G)])
                    nc.vector.tensor_copy(stage_f[h][:, 0, :], local[:, bass.ds(at, G)]).then_inc(lay.scal, 1)
                    dve.wait_ge(lay.scal, it * 2 + (h + 1))
                    for j in range(G):
                        if k < 2:
                            last = nc.vector.tensor_scalar(hot[h][:, j, :], iota[:, 0:P], stage_f[h][:, 0, j:j + 1],
                                                           stage_f[h][:, 1, j:j + 1], ALU.is_equal, ALU.mult)
                            last = nc.vector.tensor_scalar(hotb[h][:, j, :], iotab[:, :], stage_f[h][:, 2, j:j + 1], None, ALU.is_equal)
                        else:
                            last = nc.vector.tensor_scalar(hot[h][:, j, :], iota[:, 0:P], stage_f[h][:, 0, j:j + 1], None, ALU.is_equal)
                    if k < 2:
                        last = nc.vector.tensor_tensor(hot_hi[h][:, :, :], iota[:, 0:NW].unsqueeze(1).broadcast_to([P, G, NW]),
                                                       stage_f[h][:, 3, :].unsqueeze(2).broadcast_to([P, G, NW]), ALU.is_equal)
                    last.then_inc(lay.hots, 1)
            dve.wait_ge(lay.done, 1)

        def windows(first, n):
            return slice(first, first + n)

        def update_dve(dve, steps, k):
            after = steps.after
            lay = L[k]
            if k == 0:
                nc.vector.tensor_copy(hcount[:, 0:NW], work[:, 0:NW])
            if k == 1:
                nc.vector.tensor_copy(hcount[:, NW:2 * NW], work[:, NW:2 * NW])
            for b in range(ACC_BANKS):
                n = min(WPB, NW - WPB * b)
                ws = slice(WPB * b, WPB * b + n)
                a = acc[:, b * BANK:b * BANK + n * AW].rearrange("p (w c) -> p w c", c=AW)[:, :, 0:D]
                if k == 0:
                    ins = nc.vector.tensor_tensor(xs[:, ws, :], xs[:, ws, :], a, ALU.add)
                elif k == 1:
                    ins = nc.vector.scalar_tensor_tensor(xs[:, ws, :], a, 0.0, xs[:, ws, :], ALU.max, ALU.add)
                else:
                    nc.vector.tensor_tensor(cat[:, ws, D:P], a, hs[:, ws, :], ALU.mult)
                    ins = nc.vector.tensor_copy(cat[:, ws, 0:D], a)
                after(ins)
            dve.sem_inc(s_taken_acc, 1)
            if k == 2:
                dve.sem_inc(s_cat, 1)
                for w in range(NW):
                    dve.wait_ge(s_catp, w + 1)
                    nc.vector.tensor_copy(kvT[:, w * P:(w + 1) * P], bank(w % 2)[:, 0:P]).then_inc(s_catT, 1)
                    if w >= 1:
                        add_combined(dve, steps, w - 1)
                add_combined(dve, steps, NW - 1)

        def add_combined(dve, steps, w):
            dve.wait_ge(s_comb, w + 1)
            nc.vector.scalar_tensor_tensor(xs[:, w, :], bank(2 + w % 2)[:, 0:D], hist[:, 1, w:w + 1],
                                           xs[:, w, :], ALU.mult, ALU.add).then_inc(s_added, 1)
            if w == NW - 1:
                dve.wait_ge(s_added, NW)

        def node3_pe(pe):
            lay = L[3]
            pe.wait_ge(s_weights3, 16 * W3)
            pe.wait_ge(s_added, NW)
            for r in range(R3):
                last = nc.tensor.transpose(bank(2)[0:D, r * D:(r + 1) * D], att[:, r, :], ident[0:D, 0:D])
            last.then_inc(s_attp, 1)
            pe.wait_ge(s_attT, 1)
            for r in range(R3):
                last = nc.tensor.matmul(bank(3)[0:D, r * D:(r + 1) * D], attT[:, r, :], attT[:, r, :], start=True, stop=True)
            last.then_inc(s_relp, 1)
            pe.wait_ge(lay.norm, 1)
            turn_pe(pe, lay, P, lambda w: twice[:, w, :])
            pe.wait_ge(s_hm, 1)
            for c in range(-(-NP // BANK)):
                n = min(BANK, NP - c * BANK)
                if c >= 2:
                    pe.wait_ge(s_kv, c - 1)
                for j in range(2):
                    last = nc.tensor.matmul(bank(c % 2)[:, 0:n], wkv_sb[:, j, :], hm[j][:, c * BANK:c * BANK + n], start=(j == 0), stop=(j == 1))
                last.then_inc(s_kvp, 1)
            typed_pe(pe, wq_sb, s_qp, s_qn)
            pe.wait_ge(s_kv, -(-NP // BANK))
            pe.wait_ge(s_rel, 1)
            for w in range(NW):
                if w < 2:
                    pe.wait_ge(s_qn, -(-NW // 8))
                else:
                    pe.wait_ge(lay.taken, w - 1)
                for c in range(2):
                    last = nc.tensor.matmul(bank((w % 2) * 2 + c), kvT[:, w * P:(w + 1) * P], rel3[:, c * 4:(c + 1) * 4, :].rearrange("i r o -> i (r o)"), start=True, stop=True)
                last.then_inc(lay.made, 1)

        def typed_pe(pe, weights, in_psum, in_sbuf):
            for w in range(NW):
                if w % 8 == 0 and w >= 16:
                    pe.wait_ge(in_sbuf, w // 8 - 1)
                for j in range(2):
                    last = nc.tensor.matmul(bank(2 + w // 8 % 2)[:, (w % 8) * D:(w % 8 + 1) * D], hm[j][:, w * P:(w + 1) * P], weights[:, j, :], start=(j == 0), stop=(j == 1))
                if w % 8 == 7 or w == NW - 1:
                    last.then_inc(in_psum, 1)

        def masked_dve(dve, steps, n):
            after = steps.after
            dve.wait_ge(s_types, 16 * n)
            after(nc.vector.tensor_copy(typeT[:, 0:N], types_i[:, 0:N]))
            after(nc.vector.memset(typeT[:, N:NP], -1.0))
            for g in range(-(-NW // 4)):
                cols = min(4, NW - 4 * g) * P
                lay_turned, lay_sb = turned3[n - 1]
                dve.wait_ge(lay_turned, g + 1)
                nc.vector.tensor_copy(hT2[:, g * 4 * P:g * 4 * P + cols], bank(g % 2)[:, 0:cols]).then_inc(lay_sb, 1)
            dve.wait_ge(lay_sb, -(-NW // 4))
            for j in range(2):
                after(nc.vector.scalar_tensor_tensor(hm[j], typeT, half[:, j:j + 1], hT2, ALU.is_equal, ALU.mult))
            dve.sem_inc(s_hm, 1)

        s_turned2, s_turned2_sb = sem("s_turned2"), sem("s_turned2_sb")
        turned3 = [(L[3].turned, L[3].turned_sb), (s_turned2, s_turned2_sb)]

        def twice_dve(dve, steps):
            for i in range(2):
                steps.after(nc.vector.tensor_copy(twice[:, :, i * D:(i + 1) * D], hs[:, :, :]))

        def node3_dve(dve, steps):
            after = steps.after
            lay = L[3]
            dve.sem_inc(s_free3, 1)
            dve.wait_ge(s_attp, 1)
            nc.vector.tensor_copy(attT[:, :, :].rearrange("p r d -> p (r d)"), bank(2)[0:D, :]).then_inc(s_attT, 1)
            dve.wait_ge(s_relp, 1)
            after(nc.vector.scalar_tensor_tensor(rel3[0:D, :, 0:D], bank(3)[0:D, :].rearrange("p (r d) -> p r d", d=D), float(HS) ** -0.5,
                                                 pri[:, :].unsqueeze(2).broadcast_to([D, R3, D]), ALU.mult, ALU.mult))
            dve.sem_inc(s_rel, 1)
            norm_dve(dve, steps, 3)
            twice_dve(dve, steps)
            dve.sem_inc(lay.norm, 1)
            masked_dve(dve, steps, 1)
            for c in range(-(-NP // BANK)):
                n = min(BANK, NP - c * BANK)
                dve.wait_ge(s_kvp, c + 1)
                nc.vector.tensor_copy(kvT[:, c * BANK:c * BANK + n], bank(c % 2)[:, 0:n]).then_inc(s_kv, 1)
            for g in range(-(-NW // 8)):
                n = min(8, NW - 8 * g) * D
                dve.wait_ge(s_qp, g + 1)
                nc.vector.tensor_copy(qn[:, g * 8 * D:g * 8 * D + n], bank(2 + g % 2)[:, 0:n]).then_inc(s_qn, 1)
            for w in range(NW):
                dve.wait_ge(lay.made, w + 1)
                if w >= 2:
                    dve.wait_ge(lay.stored[w % 2], 16 * (w // 2))
                nc.vector.tensor_copy(evac[w % 2][:, :], work[:, (w % 2) * 2 * BANK:(w % 2 + 1) * 2 * BANK]).then_inc(lay.taken, 1)
            dve.wait_ge(s_qn, -(-NW // 8))

        def scores_dve(dve, steps):
            lay = L[3]
            after = steps.after

            def front(g, first, second):
                if not (first or second):
                    dve.wait_ge(s_farm, g.n - 1)
                dve.wait_ge(s_free[g.half], g.turn + 1)
                dve.sem_inc(dve_held, 1)
                nc.vector.tensor_copy(stage_row[g.half][:, 0:G3], row8[:, bass.ds(g.n * G3, G3)]).then_inc(lay.staged, 1)
                nc.vector.tensor_copy(stage_f[g.half][:, 0, 0:G3], local[:, bass.ds(g.n * G3, G3)]).then_inc(P1.scal, 1)
                dve.wait_ge(P1.scal, g.n + 1)
                for j in range(G3):
                    last = nc.vector.tensor_scalar(hot3b[g.half][:, j, :], iotab[:, :], stage_f[g.half][:, 0, j:j + 1], None, ALU.is_equal)
                last.then_inc(P1.hots, 1)

            def middle(g, first):
                dve.wait_ge(lay.gathered[g.half], (g.turn + 1) * (16 * G3))
                dve.sem_inc(dve_held, 1)
                dve.wait_ge(P1.picked, g.n + 1)
                nc.vector.tensor_tensor(prod[:, :, :], rows3[g.half][:, :, 0:D], bank(2).rearrange("p (g d) -> p g d", d=D), ALU.mult).then_inc(P1.used, 1)
                dve.wait_ge(P1.used, g.n + 1)
                after(nc.vector.tensor_reduce(a_g[:, 0, :], prod[:, :, :].rearrange("p g (h d) -> p (g h) d", d=HS), AX_X, ALU.add))
                nc.vector.tensor_scalar(score[:, bass.ds(g.n * (G3 * H), G3 * H)], a_g[:, 0, :], 1.0, None, ALU.mult)
                if not first:
                    dve.wait_ge(s_partsp, g.n)
                for i in range(3):
                    after(nc.vector.tensor_copy(a_parts[:, i, :], a_g[:, i, :]))
                    if i < 2:
                        after(nc.vector.tensor_tensor(a_g[:, i + 1, :], a_g[:, i, :], a_parts[:, i, :], ALU.subtract))
                dve.sem_inc(s_parts, 1)

            def back(g):
                for j in range(G3):
                    dve.wait_ge(s_mx, g.n * G3 + (j + 1))
                    nc.vector.tensor_reduce(max_g[:, j, :], acc[:, (j % 4) * BANK:(j % 4 + 1) * BANK].rearrange("p (h e) -> p h e", e=P), AX_X, ALU.max).then_inc(s_red, 1)
                dve.wait_ge(s_red, g.n * G3 + G3)
                after(nc.vector.tensor_scalar(tile_max[:, bass.ds(g.n * (G3 * H), G3 * H)], max_g[:, :, :].rearrange("p g h -> p (g h)"), 1.0, None, ALU.mult))

            def own_far(g):
                for j in range(G3):
                    last = nc.vector.tensor_scalar(far[:, j, :], iotab[:, :], stage_f[g.half][:, 0, j:j + 1], -FAR, ALU.not_equal, ALU.mult)
                last.then_inc(s_farm, 1)

            def step(g, first=False, last=False):
                if not last:
                    front(g.next(), False, first)
                middle(g, first)
                if not first:
                    back(g.prev())
                own_far(g)

            front(Group(0, 0), True, False)
            pipeline(dve, step, steps, 2 * 7)
            back(Group(NG3 // 2 - 1, 1))

        def scores_pe(pe):
            def front(g, first, second):
                offsets = load_offsets(pe, q_off, g, (NW - 1) * D)
                pe.wait_ge(P1.hots, g.n + 1)
                if not (first or second):
                    pe.wait_ge(P1.hotT, g.n - 1)
                tp = bank(g.half).bitcast(BF16).rearrange("p (g e) -> p g e", e=P)
                for j in range(G3):
                    last = nc.tensor.transpose(tp[:, j, :], hot3b[g.half][:, j, :], identb[:, :])
                last.then_inc(P1.tp, 1)
                pe.wait_ge(P1.hotT, g.n + 1)
                if not first:
                    pe.wait_ge(P1.used, g.n)
                pe.sem_inc(pe_held, 1)
                for j in range(G3):
                    last = nc.tensor.matmul(bank(2)[:, j * D:(j + 1) * D], hotT[g.half][:, j, :], qn[:, bass.ds(offsets[j], D)], start=True, stop=True)
                last.then_inc(P1.picked, 1)

            def own(g, first):
                pe.wait_ge(s_parts, g.n + 1)
                if not first:
                    pe.wait_ge(s_partsT, g.n)
                nc.tensor.transpose(bank(3).bitcast(BF16)[0:3 * G3 * H, 0:P], a_parts[:, :, :].rearrange("p s c -> p (s c)"), identb[:, :]).then_inc(s_partsp, 1)
                pe.wait_ge(s_farm, g.n + 1)
                pe.wait_ge(s_partsT, g.n + 1)
                for j in range(G3):
                    if not first or j >= 4:
                        pe.wait_ge(s_red, g.n * G3 + (j - 3))
                    o = acc[:, (j % 4) * BANK:(j % 4 + 1) * BANK]
                    nc.tensor.matmul(o, far[:, j, :], identb[:, :].unsqueeze(1).broadcast_to([P, H, P]), start=True, stop=False, skip_group_check=True)
                    for h in range(H):
                        last = nc.tensor.matmul(o[:, h * P:(h + 1) * P], sel[:, j * H + h:j * H + h + 1].broadcast_to([3 * G3 * H, P]), partsT[g.half][:, :],
                                                start=False, stop=(h == H - 1), skip_group_check=True)
                    last.then_inc(s_mx, 1)

            def step(g, first=False, last=False):
                if not last:
                    front(g.next(), False, first)
                own(g, first)

            pe.wait_ge(s_qn, -(-NW // 8))
            pe.wait_ge(L[3].taken, NW)
            front(Group(0, 0), True, False)
            pipeline(pe, step)

        def scores_act(act):
            def front(g, first, second):
                act.wait_ge(P1.tp, g.n + 1)
                if not (first or second):
                    act.wait_ge(P1.picked, g.n - 1)
                nc.scalar.activation(hotT[g.half].rearrange("p g e -> p (g e)"), bank(g.half).bitcast(BF16), ACT.Copy).then_inc(P1.hotT, 1)

            def step(g, first=False, last=False):
                if not last:
                    front(g.next(), False, first)
                act.wait_ge(s_partsp, g.n + 1)
                if not first:
                    act.wait_ge(s_mx, g.n * G3 - G3) if not g.second() else None
                nc.scalar.activation(partsT[g.half][:, :], bank(3).bitcast(BF16)[0:3 * G3 * H, 0:P], ACT.Copy).then_inc(s_partsT, 1)

            front(Group(0, 0), True, False)
            pipeline(act, step)

        def scores_sp(sp):
            for h in range(2):
                sp.sem_inc(s_free[h], 1)
            with sp.Fori(0, NG3 // 2) as it:
                for h in range(2):
                    sp.wait_ge(L[3].gathered[h], (it + 1) * (16 * G3))
                    sp.dma_start(messages[bass.ds(it * 2 + h, 1)].rearrange("o p (g d) -> p (o g) d", d=D), rows3[h][:, :, D:2 * D]).then_inc(s_spill[h], 16)
                    sp.wait_ge(s_spill[h], (it + 1) * 16)
                    sp.sem_inc(s_free[h], 1)

        def scores_pool(pool):
            lay = L[3]
            for i in range(2):
                pool.wait_ge(lay.stored[i], 16 * ((NW + 1 - i) // 2))
            with pool.Fori(0, NG3 // 2) as it:
                for h in range(2):
                    pool.wait_ge(lay.staged, it * 2 + (h + 1))
                    pool.sem_inc(pool_held, 1)
                    for j in range(G3):
                        pool.indirect_dma_start(rows3[h][:, j, :], None, table3,
                                                bass.IndirectOffsetOnAxis(stage_row[h][:, j:j + 1], 0)).then_inc(lay.gathered[h], 16)

        def maxima_dve(dve, steps):
            after = steps.after
            for h in range(2):
                dve.wait_ge(s_free[h], NG3 // 2 + 1)
            after(nc.vector.memset(change[:, :, :], 0.0))
            after(nc.vector.tensor_tensor(change[:, 0, 1:T], winrow[:, 1:T], winrow[:, 0:T - 1], ALU.not_equal))
            after(nc.vector.tensor_scalar(change[:, 0, :], change[:, 0, :], -FAR, None, ALU.mult))
            after(nc.vector.tensor_copy(change[:, 1, 0:T - 1], change[:, 0, 1:T]))
            tm = tile_max.rearrange("p (t h) -> p t h", h=H)
            fm = fwd.rearrange("p (t h) -> p t h", h=H)
            for h in range(H):
                after(nc.vector.tensor_tensor_scan(fm[:, :, h], change[:, 0, :], tm[:, :, h], -FAR, ALU.add, ALU.max))
            for h in range(H):
                after(nc.vector.tensor_tensor_scan(tm[:, ::-1, h], change[:, 1, ::-1], fm[:, ::-1, h], -FAR, ALU.add, ALU.max))
            dve.sem_inc(s_maxima, 1)

        def sums_dve(dve, steps):
            def front(g, first, second):
                if not (first or second):
                    dve.wait_ge(s_sum, g.n - 1)
                dve.sem_inc(dve_held, 1)
                nc.vector.tensor_copy(stage_f[g.half][:, 0, 0:G3], local[:, bass.ds(g.n * G3, G3)]).then_inc(P2.scal, 1)
                dve.wait_ge(P2.scal, g.n + 1)
                for j in range(G3):
                    nc.vector.tensor_scalar(hot3[g.half][:, j, :], iota[:, 0:P], stage_f[g.half][:, 0, j:j + 1], None, ALU.is_equal)
                    last = nc.vector.tensor_scalar(hot3b[g.half][:, j, :], iotab[:, :], stage_f[g.half][:, 0, j:j + 1], None, ALU.is_equal)
                last.then_inc(P2.hots, 1)

            def step(g, first=False, last=False):
                dve.wait_ge(P2.picked, g.n + 1)
                nc.vector.tensor_tensor(diff[g.half][:, :], score[:, bass.ds(g.n * (G3 * H), G3 * H)], bank(2 + g.half)[:, 0:G3 * H], ALU.subtract).then_inc(s_diff, 1)
                if not last:
                    front(g.next(), False, first)
                dve.wait_ge(s_exp, g.n + 1)
                dve.sem_inc(dve_held, 1)
                dve.wait_ge(s_msg_in[g.half], (g.turn + 1) * 16)
                nc.vector.tensor_tensor(msg[g.half][:, :, 0:D].rearrange("p g (h d) -> p g h d", d=HS), msg_in[g.half].rearrange("p g (h d) -> p g h d", d=HS),
                                        msg[g.half][:, :, D:AW].unsqueeze(3).broadcast_to([P, G3, H, HS]), ALU.mult).then_inc(s_msg, 1)

            front(Group(0, 0), True, False)
            pipeline(dve, step)
            dve.wait_ge(L[3].done, 1)

        def sums_pe(pe):
            pe.wait_ge(s_red, T)
            for b in range(ACC_BANKS):
                last = nc.tensor.matmul(acc[:, b * BANK:(b + 1) * BANK], identb[:, :], zeros[:, :], start=True, stop=False, skip_group_check=True)
            pe.wait_ge(s_maxima, 1)

            def front(g, first, second):
                pe.wait_ge(P2.hots, g.n + 1)
                if not (first or second):
                    pe.wait_ge(P2.hotT, g.n - 1)
                tp = bank(g.half).bitcast(BF16).rearrange("p (g e) -> p g e", e=P)
                for j in range(G3):
                    last = nc.tensor.transpose(tp[:, j, :], hot3b[g.half][:, j, :], identb[:, :])
                last.then_inc(P2.tp, 1)
                pe.wait_ge(P2.hotT, g.n + 1)
                if not (first or second):
                    pe.wait_ge(s_diff, g.n - 1)
                pe.sem_inc(pe_held, 1)
                for j in range(G3):
                    last = nc.tensor.matmul(bank(2 + g.half)[:, j * H:(j + 1) * H], hotT[g.half][:, j, :], tile_max[:, bass.ds(g.n * (G3 * H) + j * H, H)], start=True, stop=True)
                last.then_inc(P2.picked, 1)

            def step(g, first=False, last=False):
                if not last:
                    front(g.next(), False, first)
                offsets = load_offsets(pe, acc_off, g, acc_at(NW - 1))
                pe.wait_ge(s_msg, g.n + 1)
                pe.sem_inc(pe_held, 1)
                for j in range(G3):
                    last_ = nc.tensor.matmul(acc[:, bass.ds(offsets[j], AW)], hot3[g.half][:, j, :], msg[g.half][:, j, :], start=False, stop=False, skip_group_check=True)
                last_.then_inc(s_sum, 1)

            front(Group(0, 0), True, False)
            pipeline(pe, step)
            for b in range(ACC_BANKS):
                last = nc.tensor.matmul(acc[:, b * BANK:b * BANK + 1], identb[:, :], zeros[:, 0:1], start=False, stop=True, skip_group_check=True)
            last.then_inc(L[3].done, 1)

        def sums_act(act):
            def front(g, first, second):
                act.wait_ge(P2.tp, g.n + 1)
                if not (first or second):
                    act.wait_ge(P2.picked, g.n - 1)
                nc.scalar.activation(hotT[g.half].rearrange("p g e -> p (g e)"), bank(g.half).bitcast(BF16), ACT.Copy).then_inc(P2.hotT, 1)

            def step(g, first=False, last=False):
                act.wait_ge(s_diff, g.n + 1)
                if not (first or g.second()):
                    act.wait_ge(s_sum, g.n - 1)
                nc.scalar.activation(msg[g.half][:, :, D:AW], diff[g.half].rearrange("p (g h) -> p g h", h=H), ACT.Exp).then_inc(s_exp, 1)
                if not last:
                    front(g.next(), False, first)

            front(Group(0, 0), True, False)
            pipeline(act, step)

        def sums_sp(sp):
            def load(g):
                sp.dma_start(msg_in[g.half].rearrange("p g d -> p (g d)"), messages[bass.ds(g.n, 1)].rearrange("o p c -> p (o c)")).then_inc(s_msg_in[g.half], 16)

            sp.wait_ge(s_maxima, 1)
            for h in range(2):
                load(Group(0, h))
            with sp.Fori(1, NG3 // 2) as it:
                for h in range(2):
                    g = Group(it, h)
                    sp.wait_ge(s_msg, g.n - 1)
                    load(g)

        def output3_dve(dve, steps):
            after = steps.after
            dve.sem_inc(s_free3, 1)
            for b in range(ACC_BANKS):
                n = min(WPB, NW - WPB * b)
                ws = slice(WPB * b, WPB * b + n)
                a = acc[:, b * BANK:b * BANK + n * AW].rearrange("p (w c) -> p w c", c=AW)
                nc.vector.tensor_scalar(den[:, ws, :], a[:, :, D:AW], 1.0e-30, None, ALU.max)
                after(nc.vector.tensor_copy(cs[:, ws, :], a[:, :, 0:D]))
            after(nc.vector.reciprocal(den[:, :, :], den[:, :, :]))
            after(nc.vector.tensor_tensor(hs[:, :, :].rearrange("p w (h d) -> p (w h) d", d=HS), cs[:, :, :].rearrange("p w (h d) -> p (w h) d", d=HS),
                                          den[:, :, :].rearrange("p w h -> p (w h)").unsqueeze(2).broadcast_to([P, NW * H, HS]), ALU.mult))
            twice_dve(dve, steps)
            dve.sem_inc(s_twice2, 1)
            masked_dve(dve, steps, 2)
            for g in range(-(-NW // 8)):
                n = min(8, NW - 8 * g)
                dve.wait_ge(s_outp, g + 1)
                nc.vector.tensor_tensor(xs[:, 8 * g:8 * g + n, :], xs[:, 8 * g:8 * g + n, :], bank(2 + g % 2)[:, 0:n * D].rearrange("p (w d) -> p w d", d=D), ALU.add).then_inc(s_outx, 1)
            dve.wait_ge(s_outx, -(-NW // 8))

        def output3_pe(pe):
            pe.wait_ge(s_twice2, 1)
            turn_pe(pe, Turned2, P, lambda w: twice[:, w, :])
            pe.wait_ge(s_hm, 2)
            typed_pe(pe, wa_sb, s_outp, s_outx)

        class Turned2:
            turned, turned_sb = turned3[1]

        s_twice2 = sem("s_twice2")

        def load_offsets(pe, table, g, most):
            _, offsets = nc.values_load_multi_w_load_instructions(
                table[0:1, bass.ds(g.n * G3, G3)], engines=[pe.engine], min_val=0, max_val=most,
                skip_runtime_bounds_check_because="tiles' windows are below NW")
            return offsets

        def pipeline(engine, step, steps=None, per=0):
            turns = NG3 // 2
            step(Group(0, 0), first=True)
            step(Group(0, 1))
            with engine.Fori(1, turns - 1) as it:
                if steps:
                    steps.enter(it, per, 1)
                step(Group(it, 0))
                step(Group(it, 1))
                if steps:
                    steps.leave(turns - 2, 1)
            step(Group(turns - 1, 0))
            step(Group(turns - 1, 1), last=True)

        @block.sync
        def _(sp):
            sp.wait_ge(s_clear, 1)
            for a, b in ((dst, raw_dst), (src, raw_src), (edge_type_8, raw_t8),
                         (edge_type_16, raw_t16), (edge_weight1.rearrange("e o -> (e o)"), raw_w)):
                sp.dma_start(b[0:P - 1, :], a[0:(P - 1) * EC].rearrange("(p c) -> p c", c=EC)).then_inc(s_edges, 16)
                sp.dma_start(b[P - 1:P, 0:LASTP], a[(P - 1) * EC:E].rearrange("(p c) -> p c", p=1)).then_inc(s_edges, 16)
            sp.wait_ge(s_starts, 1)
            sp.wait_ge(s_sorted, 1)
            load_tiles(sp, 0)
            for k, (lay, piece) in enumerate(((L[0], 0), (L[1], 1))):
                if layers > k:
                    table, width = ((table0, R0 * D), (table1, R1 * D))[k]
                    store_table(sp, lay, table, width)
            if layers > 2:
                sp.wait_ge(L[2].norm, 1)
                sp.dma_start(table2.rearrange("(w p) d -> p w d", p=P), hs[:, :, :]).then_inc(L[2].stored[0], 16)
            if layers > 3:
                def types():
                    sp.dma_start(types_i[:, 0:N], node_type_4.partition_broadcast(P)).then_inc(s_types, 16)

                sp.wait_ge(s_free3, 1)
                types()
                store_table(sp, L[3], table3, R3 * 2 * D)
                scores_sp(sp)
                sums_sp(sp)
                sp.wait_ge(s_free3, 2)
                types()
            finish(sp)

        @block.scalar
        def _(act):
            act.wait_ge(s_clear, 2)
            act.dma_start(xs[:, 0:NW - 1, :], x[0:(NW - 1) * P, :].rearrange("(w p) d -> p w d", p=P)).then_inc(s_nodes, 16)
            act.dma_start(xs[0:LASTN, NW - 1, :], x[(NW - 1) * P:N, :]).then_inc(s_nodes, 16)
            act.dma_start(w0_sb[:, :, :], w0.rearrange("r i o -> i r o")).then_inc(s_weights, 16)
            act.dma_start(w1_sb[:, :, :], w1.rearrange("r i o -> i r o")).then_inc(s_weights, 16)
            act.dma_start(loop_sb[:, :], loop0).then_inc(s_weights, 16)
            act.dma_start(bias_sb[:, :], bias0.partition_broadcast(P)).then_inc(s_weights, 16)
            act.dma_start(w2_sb[0:D, :], w2a).then_inc(s_weights, 16)
            act.dma_start(w2_sb[D:P, :], w2b).then_inc(s_weights, 16)
            act.wait_ge(s_starts, 1)
            act.wait_ge(s_sorted, 1)
            load_tiles(act, 1)
            act.wait_ge(s_clear3, 1)
            for i in range(2):
                rows = slice(i * D, (i + 1) * D)
                for weights, o, cols in ((wk, wkv_sb, slice(0, D)), (wv, wkv_sb, slice(D, P)), (wq, wq_sb, slice(0, D)), (wa, wa_sb, slice(0, D))):
                    act.dma_start(o[rows, :, cols], weights.rearrange("(j i) r c -> i r j c", i=2)[i]).then_inc(s_weights3, 16)
            for h in range(H):
                rows = slice(h * HS, (h + 1) * HS)
                act.dma_start(att[rows, :, h * HS:(h + 1) * HS], rel_att[h].rearrange("r d o -> d r o")).then_inc(s_weights3, 16)
                act.dma_start(rel3[D + h * HS:D + (h + 1) * HS, :, D + h * HS:D + (h + 1) * HS], rel_msg[h].rearrange("r d o -> d r o")).then_inc(s_weights3, 16)
                act.dma_start(pri[rows, :], rel_pri[h].partition_broadcast(HS)).then_inc(s_weights3, 16)
            for k in range(min(layers, 4)):
                node_act(act, k)
            if layers > 3:
                scores_act(act)
                sums_act(act)

        @block.gpsimd
        def _(pool):
            pool.iota(iota_i[:, :], [[1, T]], base=0, channel_multiplier=0).then_inc(s_pool, 1)
            pool.iota(part_i[:, :], [[0, 1]], base=0, channel_multiplier=1).then_inc(s_pool, 1)
            pool.memset(ident[:, :], 0.0).then_inc(s_pool, 1)
            pool.memset(before[:, :], 0.0).then_inc(s_pool, 1)
            pool.memset(ones[:, :], 1.0).then_inc(s_pool, 1)
            pool.memset(zeros[:, :], 0.0).then_inc(s_pool, 1)
            pool.memset(far_edges[:, :, :], 0).then_inc(s_pool, 1)
            pool.memset(att[:, :, :], 0.0).then_inc(s_pool, 1)
            pool.memset(rel3[:, :, :], 0.0).then_inc(s_pool, 1)
            pool.wait_ge(s_pool, 9)
            pool.sem_inc(s_clear3, 1)
            pool.memset(far_edges[:, :, 3:4], NW * P).then_inc(s_pool, 1)
            pool.affine_select(out=ident[:, :], in_=ident[:, :], compare_op=ALU.not_equal, fill=1.0,
                               base=0, pattern=[[-1, P]], channel_multiplier=1).then_inc(s_pool, 1)
            pool.affine_select(out=before[:, :], in_=before[:, :], compare_op=ALU.is_ge, fill=1.0,
                               base=0, pattern=[[-1, P]], channel_multiplier=1).then_inc(s_pool, 1)
            pool.wait_ge(s_pool, 12)
            pool.sem_inc(s_const, 1)
            pool.dma_start(records[EC * P:T * P, :].rearrange("(p c) r -> p (c r)", p=P),
                           far_edges[:, :, :].rearrange("p c r -> p (c r)")).then_inc(s_far, 16)
            with pool.Fori(0, EC // (2 * RB)) as it:
                for h in range(2):
                    pool.wait_ge(s_recst, it * 2 + (h + 1))
                    pool.sem_inc(pool_held, 1)
                    for j in range(RB):
                        pool.indirect_dma_start(records, bass.IndirectOffsetOnAxis(stage_row[h][:, j:j + 1], 0),
                                                stage_rec[h][:, j, :], None).then_inc(s_recout[h], 16)
            for h in range(2):
                pool.wait_ge(s_recout[h], 16 * EC // 2)
            pool.wait_ge(s_far, 16)
            pool.sem_inc(s_sorted, 1)
            for k in range(min(layers, 3)):
                gather_rows(pool, k)
            if layers > 3:
                scores_pool(pool)

        @block.tensor
        def _(pe):
            pe.wait_ge(s_const, 1)
            pe.wait_ge(s_totals, 1)
            nc.tensor.matmul(work[:, 0:NB], before[:, :], totals[:, :], start=True, stop=True)
            nc.tensor.matmul(work[0:NB, BANK:BANK + 1], totals[:, :], ones[:, 0:1], start=True, stop=True).then_inc(s_off, 1)
            pe.wait_ge(s_cnt, 1)
            nc.tensor.matmul(work[:, 2 * BANK:2 * BANK + NB], small[0:NB, 0:1].broadcast_to([NB, P]), before[0:NB, 0:NB], start=True, stop=True)
            nc.tensor.matmul(work[0:NB, 3 * BANK:3 * BANK + 1], before[0:NB, 0:NB], small[0:NB, 1:2], start=True, stop=True).then_inc(s_tiles, 1)
            pe.wait_ge(s_geq, 1)
            for c in range(2):
                cols = slice(c * HALF_T, (c + 1) * HALF_T)
                nc.tensor.matmul(work[:, c * BANK:c * BANK + HALF_T], deltab[0:NW, 0:P], geq[0:NW, cols], start=True, stop=True)
                last = nc.tensor.matmul(work[:, (2 + c) * BANK:(2 + c) * BANK + HALF_T], small[0:NW, 4:5].broadcast_to([NW, P]), geq[0:NW, cols], start=True, stop=True)
            last.then_inc(s_win, 1)
            for k in range(min(layers, 3)):
                node_pe(pe, k)
                edge_pe(pe, k)
            if layers > 2:
                combine_pe(pe)
            if layers > 3:
                node3_pe(pe)
                scores_pe(pe)
                sums_pe(pe)
                output3_pe(pe)

        @block.vector
        def _(dve):
            steps = Steps(dve, s_dve)
            dve.memset(raw_dst, NW * P).then_inc(s_dve, 1)
            for a in (raw_src, raw_t8, raw_t16):
                dve.memset(a, 0).then_inc(s_dve, 1)
            dve.memset(raw_w, 0.0).then_inc(s_dve, 1)
            dve.wait_ge(s_dve, 5)
            dve.sem_inc(s_clear, 1)
            dve.memset(xs[:, NW - 1, :], 0.0).then_inc(s_dve, 1)
            dve.memset(src_hi[:, :], -1.0).then_inc(s_dve, 1)
            dve.memset(src_lo[:, :], 0.0).then_inc(s_dve, 1)
            dve.memset(dst_hi[:, :], -1.0).then_inc(s_dve, 1)
            dve.memset(dst_lo[:, :], 0.0).then_inc(s_dve, 1)
            dve.wait_ge(s_dve, 10)
            dve.sem_inc(s_clear, 1)
            steps.done = 10
            after = steps.after
            dve.wait_ge(s_const, 1)
            after(nc.vector.tensor_copy(iota[:, :], iota_i[:, :]))
            after(nc.vector.tensor_copy(part[:, :], part_i[:, :]))
            after(nc.vector.tensor_copy(iotab[:, :], iota[:, 0:P]))
            after(nc.vector.tensor_copy(identb[:, :], ident[:, :]))
            after(nc.vector.tensor_scalar(half[:, 0:1], part[:, :], float(D), None, ALU.is_ge))
            after(nc.vector.tensor_scalar(half[:, 1:2], half[:, 0:1], 2.0, None, ALU.add))
            K = G3 * H
            after(nc.vector.tensor_tensor(sel[:, :], ident[0:3 * K, 0:K], ident[0:3 * K, K:2 * K], ALU.add))
            after(nc.vector.tensor_tensor(sel[:, :], sel[:, :], ident[0:3 * K, 2 * K:3 * K], ALU.add))
            dve.sem_inc(s_identb, 1)

            dve.wait_ge(s_edges, 16 * 10)
            after(nc.vector.tensor_scalar(win_i, raw_dst, 7, None, ALU.arith_shift_right))
            after(nc.vector.tensor_copy(win, win_i))
            nc.vector.scalar_tensor_tensor(recs_in[:, :, 0], raw_src, float(R0), raw_t8, ALU.mult, ALU.add)
            nc.vector.scalar_tensor_tensor(recs_in[:, :, 1], raw_src, float(R1), raw_t16, ALU.mult, ALU.add)
            nc.vector.tensor_copy(recs_in[:, :, 2].bitcast(F32), raw_w)
            after(nc.vector.tensor_copy(recs_in[:, :, 3], raw_dst))
            after(nc.vector.tensor_copy(dst_hi[:, 0:EC], win))
            after(nc.vector.tensor_scalar(pos_i, raw_dst, P - 1, None, ALU.bitwise_and))
            after(nc.vector.tensor_copy(dst_lo[:, 0:EC], pos_i))
            after(nc.vector.tensor_scalar(pos_i, raw_src, P - 1, None, ALU.bitwise_and))
            after(nc.vector.tensor_copy(src_lo[:, 0:EC], pos_i))
            after(nc.vector.tensor_scalar(pos_i, raw_src, 7, None, ALU.arith_shift_right))
            after(nc.vector.tensor_copy(src_hi[:, 0:EC], pos_i))
            after(nc.vector.tensor_scalar(isb, win, float(NW), 1000.0, ALU.is_equal, ALU.mult))
            after(nc.vector.tensor_tensor(src_hi[:, 0:EC], src_hi[:, 0:EC], isb, ALU.add))

            with dve.Fori(0, NB) as b:
                steps.enter(b, 3)
                after(nc.vector.tensor_copy(cur[:, 0:1], iota[:, bass.ds(b, 1)]))
                after(nc.vector.tensor_scalar(isb, win, cur[:, 0:1], None, ALU.is_equal))
                after(nc.vector.tensor_reduce(totals[:, bass.ds(b, 1)], isb, AX_X, ALU.add))
                steps.leave(NB)
            dve.sem_inc(s_totals, 1)
            dve.wait_ge(s_off, 1)
            after(nc.vector.tensor_copy(offs[:, :], work[:, 0:NB]))
            after(nc.vector.tensor_copy(small[0:NB, 0:1], work[0:NB, BANK:BANK + 1]))
            after(nc.vector.tensor_scalar(small_i[0:NB, 0:1], small[0:NB, 0:1], float(P - 1), None, ALU.add))
            after(nc.vector.tensor_scalar(small_i[0:NB, 1:2], small_i[0:NB, 0:1], 7, None, ALU.arith_shift_right))
            after(nc.vector.tensor_copy(small[0:NB, 1:2], small_i[0:NB, 1:2]))
            dve.sem_inc(s_cnt, 1)
            after(nc.vector.scalar_tensor_tensor(small[0:NB, 4:5], small[0:NB, 1:2], -float(P), small[0:NB, 0:1], ALU.mult, ALU.add))
            dve.wait_ge(s_tiles, 1)
            after(nc.vector.tensor_tensor(offs[:, :], offs[:, :], work[:, 2 * BANK:2 * BANK + NB], ALU.add))
            after(nc.vector.tensor_tensor(small[0:NB, 2:3], small[0:NB, 1:2], work[0:NB, 3 * BANK:3 * BANK + 1], ALU.add))
            after(nc.vector.tensor_scalar(geq[0:NB, :], iota[0:NB, :], small[0:NB, 2:3], None, ALU.is_ge))
            nc.vector.tensor_scalar(deltab[:, :], part[:, 0:1].broadcast_to([P, P]), float(NW - 1), None, ALU.is_lt)
            after(nc.vector.tensor_scalar(small[:, 5:6], part[:, :], float(NW - 1), None, ALU.is_lt))
            after(nc.vector.tensor_tensor(small[0:NB, 4:5], small[0:NB, 4:5], small[0:NB, 5:6], ALU.mult))
            dve.sem_inc(s_geq, 1)
            dve.wait_ge(s_win, 1)
            for c in range(2):
                cols = slice(c * HALF_T, (c + 1) * HALF_T)
                nc.vector.tensor_copy(winrow[:, cols], work[:, c * BANK:c * BANK + HALF_T])
                after(nc.vector.scalar_tensor_tensor(geq[:, cols], iota[:, cols], float(P), work[:, (2 + c) * BANK:(2 + c) * BANK + HALF_T], ALU.mult, ALU.add))
            after(nc.vector.tensor_copy(start_i[:, :], geq[:, :]))
            dve.sem_inc(s_starts, 1)
            after(nc.vector.tensor_scalar(geq[:, :], winrow[:, :], float(AW), None, ALU.mult))
            for b in range(1, ACC_BANKS):
                after(nc.vector.tensor_scalar(local[:, :], winrow[:, :], float(WPB * b), float(BANK - WPB * AW), ALU.is_ge, ALU.mult))
                after(nc.vector.tensor_tensor(geq[:, :], geq[:, :], local[:, :], ALU.add))
            after(nc.vector.tensor_copy(acc_off[:, :], geq[:, :]))
            after(nc.vector.tensor_scalar(q_off[:, :], winrow[:, :], float(D), None, ALU.mult))
            after(nc.vector.memset(pos, -1.0))
            with dve.Fori(0, NB) as b:
                steps.enter(b, 6)
                after(nc.vector.tensor_copy(cur[:, 0:1], iota[:, bass.ds(b, 1)]))
                after(nc.vector.tensor_copy(cur[:, 1:2], offs[:, bass.ds(b, 1)]))
                after(nc.vector.tensor_scalar(isb, win, cur[:, 0:1], None, ALU.is_equal))
                after(nc.vector.tensor_tensor_scan(cum, isb, isb, cur[:, 1:2], ALU.add, ALU.bypass))
                after(nc.vector.tensor_tensor(picked, isb, cum, ALU.mult))
                after(nc.vector.tensor_tensor(pos, pos, picked, ALU.add))
                steps.leave(NB)
            after(nc.vector.tensor_copy(pos_i, pos))
            for h in range(2):
                nc.vector.tensor_copy(stage_row[h][:, :], pos_i[:, h * RB:(h + 1) * RB])
                after(nc.vector.tensor_copy(stage_rec[h][:, :, :], recs_in[:, h * RB:(h + 1) * RB, :]))
                dve.sem_inc(s_recst, 1)
            with dve.Fori(1, EC // (2 * RB)) as it:
                for h in range(2):
                    dve.wait_ge(s_recout[h], it * (16 * RB))
                    dve.sem_inc(dve_held, 1)
                    nc.vector.tensor_copy(stage_row[h][:, :], pos_i[:, bass.ds(it * (2 * RB) + h * RB, RB)])
                    nc.vector.tensor_copy(stage_rec[h][:, :, :], recs_in[:, bass.ds(it * (2 * RB) + h * RB, RB), :]).then_inc(s_recst, 1)

            if layers > 0:
                dve.wait_ge(s_nodes, 32)
                norm_dve(dve, steps, 0)

            for i in range(2):
                dve.wait_ge(s_recs[i], 16 * HALF_T)
            nc.vector.tensor_copy(row8[:, :], recs[:, :, 0])
            nc.vector.tensor_copy(row16[:, :], recs[:, :, 1])
            nc.vector.tensor_copy(weight[:, :], recs[:, :, 2].bitcast(F32))
            after(nc.vector.tensor_copy(local[:, :], recs[:, :, 3]))
            after(nc.vector.scalar_tensor_tensor(local[:, :], winrow[:, :], -float(P), local[:, :], ALU.mult, ALU.add))

            for k in range(min(layers, 3)):
                if k > 0:
                    norm_dve(dve, steps, k)
                if k < 2:
                    table_dve(dve, steps, k)
                else:
                    degrees_dve(dve, steps)
                edge_dve(dve, steps, k)
                update_dve(dve, steps, k)
            if layers > 3:
                node3_dve(dve, steps)
                scores_dve(dve, steps)
                maxima_dve(dve, steps)
                sums_dve(dve, steps)
                output3_dve(dve, steps)
            dve.sem_inc(s_final, 1)

_INS = ['x', 'src', 'dst', 'edge_type_16', 'edge_type_8', 'edge_weight1', 'node_type_4', 'L0_gnn_weight',
        'L0_gnn_h_bias', 'L0_gnn_loop_weight', 'L1_gnn_weight', 'L2_gnn_weight1', 'L2_gnn_weight2',
        'L3_gnn_Wk', 'L3_gnn_Wq', 'L3_gnn_Wv', 'L3_gnn_Wa', 'L3_gnn_rel_att', 'L3_gnn_rel_msg', 'L3_gnn_rel_pri']
LAYERS = 4


def kernel(**inputs):
    import numpy as _np
    import concourse.bacc as _bacc
    from concourse import mybir as _mybir
    from concourse.bass_utils import run_bass_kernel_spmd as _run

    nc = _bacc.Bacc("TRN2", target_bir_lowering=False, num_devices=1)
    arrays, args = {}, []
    for name in _INS:
        a = _np.ascontiguousarray(inputs[name])
        arrays[f"in_{name}_dram"] = a
        args.append(nc.dram_tensor(f"in_{name}_dram", a.shape, _mybir.dt.from_np(a.dtype), kind="ExternalInput").ap())
    out = nc.dram_tensor("out_0_dram", (N, D), _mybir.dt.from_np(_np.dtype("float32")), kind="ExternalOutput").ap()
    gnn_kernel(nc, *args, out, layers=LAYERS)
    r = _run(nc, [arrays], core_ids=[0])
    return r.results[0]["out_0_dram"]
```
